# Optimizing a Trainium2 kernel written in Bass

```python
import numpy as np
import jax
import jax.numpy as jnp

def _softmax(x, axis=-1):
    return jax.nn.softmax(x, axis=axis)

def _gelu(x):
    return jax.nn.gelu(x, approximate=True)

def _silu(x):
    return jax.nn.silu(x)

def _sigmoid(x):
    return jax.nn.sigmoid(x)

def _layernorm(x, axis=-1, eps=1e-05):
    m = jnp.mean(x, axis=axis, keepdims=True)
    v = jnp.var(x, axis=axis, keepdims=True)
    return (x - m) / jnp.sqrt(v + eps)

def _scatter_add(tgt, idx, src, axis=0):
    return tgt.at[idx].add(src)

def _segment_sum(src, seg, n):
    return jax.ops.segment_sum(src, seg, n)
kernel_name = 'mk_seq_preln_d1_jaxref_r8_125f78'

def setup_inputs(seed: int=0):
    np.random.seed(seed)
    _w = jnp.asarray

    def _L0_attn_setup():
        import jax, jax.numpy as jnp
        import numpy as np
        B, S, DM = (2, 256, 128)
        H, D = (16, 64)

        def _rel_pos_enc(seq_len: int, dim: int) -> jnp.ndarray:
            positions = jnp.arange(seq_len, dtype=jnp.float32)[:, None]
            div_term = jnp.exp(jnp.arange(0, dim, 2, dtype=jnp.float32) * -(np.log(10000.0) / dim))
            pe = jnp.zeros((seq_len, dim), dtype=jnp.float32)
            pe = pe.at[:, 0::2].set(jnp.sin(positions * div_term))
            pe = pe.at[:, 1::2].set(jnp.cos(positions * div_term))
            return pe
        key = jax.random.key(seed)
        k1, k2, k3 = jax.random.split(key, 3)
        x = jax.random.normal(k1, (B, S, DM), dtype=jnp.float32)
        W_qkv = jax.random.normal(k2, (DM, 3 * H * D), dtype=jnp.float32) / np.sqrt(DM)
        b_qkv = jnp.zeros((3 * H * D,), dtype=jnp.float32)
        W_out = jax.random.normal(k3, (H * D, DM), dtype=jnp.float32) / np.sqrt(H * D)
        b_out = jnp.zeros((DM,), dtype=jnp.float32)
        return {'x': x, 'W_qkv': W_qkv, 'b_qkv': b_qkv, 'W_out': W_out, 'b_out': b_out}
    _L0_attn_in = _L0_attn_setup()

    def _L0_ffn_setup():
        import jax, jax.numpy as jnp
        import numpy as np
        D_MODEL = 128
        N_HEAD = 16
        HEAD_DIM = D_MODEL // N_HEAD
        D_FF = 512
        N_EXPERTS = 4
        EPS = 1e-05

        def _layer_norm(x, gamma, beta):
            mu = jnp.mean(x, axis=-1, keepdims=True)
            var = jnp.mean((x - mu) ** 2, axis=-1, keepdims=True)
            return (x - mu) / jnp.sqrt(var + EPS) * gamma + beta
        key = jax.random.key(seed)
        ks = jax.random.split(key, 20)
        f32 = jnp.float32
        sc = 1.0 / np.sqrt(D_MODEL)
        scf = 1.0 / np.sqrt(D_FF)
        return {'src': jax.random.normal(ks[0], (4, 64, D_MODEL), f32), 'Wq': jax.random.normal(ks[1], (D_MODEL, D_MODEL), f32) * sc, 'bq': jnp.zeros((D_MODEL,), f32), 'Wk': jax.random.normal(ks[2], (D_MODEL, D_MODEL), f32) * sc, 'bk': jnp.zeros((D_MODEL,), f32), 'Wv': jax.random.normal(ks[3], (D_MODEL, D_MODEL), f32) * sc, 'bv': jnp.zeros((D_MODEL,), f32), 'Wo': jax.random.normal(ks[4], (D_MODEL, D_MODEL), f32) * sc, 'bo': jnp.zeros((D_MODEL,), f32), 'router_w': jax.random.normal(ks[5], (D_MODEL, 1), f32) * 0.05, 'router_b': jnp.zeros((1,), f32), 'W1': jax.random.normal(ks[6], (N_EXPERTS, D_MODEL, D_FF), f32) * sc, 'b1': jnp.zeros((N_EXPERTS, D_FF), f32), 'W2': jax.random.normal(ks[7], (N_EXPERTS, D_FF, D_MODEL), f32) * scf, 'b2': jnp.zeros((N_EXPERTS, D_MODEL), f32), 'ln1_g': jnp.ones((D_MODEL,), f32), 'ln1_b': jnp.zeros((D_MODEL,), f32), 'ln2_g': jnp.ones((D_MODEL,), f32), 'ln2_b': jnp.zeros((D_MODEL,), f32)}
    _L0_ffn_in = _L0_ffn_setup()
    _d = {'L0_attn_x': _L0_attn_in['x'], 'L0_attn_W_qkv': _L0_attn_in['W_qkv'], 'L0_attn_b_qkv': _L0_attn_in['b_qkv'], 'L0_attn_W_out': _L0_attn_in['W_out'], 'L0_attn_b_out': _L0_attn_in['b_out'], 'L0_ffn_Wq': _L0_ffn_in['Wq'], 'L0_ffn_bq': _L0_ffn_in['bq'], 'L0_ffn_Wk': _L0_ffn_in['Wk'], 'L0_ffn_bk': _L0_ffn_in['bk'], 'L0_ffn_Wv': _L0_ffn_in['Wv'], 'L0_ffn_bv': _L0_ffn_in['bv'], 'L0_ffn_Wo': _L0_ffn_in['Wo'], 'L0_ffn_bo': _L0_ffn_in['bo'], 'L0_ffn_router_w': _L0_ffn_in['router_w'], 'L0_ffn_router_b': _L0_ffn_in['router_b'], 'L0_ffn_W1': _L0_ffn_in['W1'], 'L0_ffn_b1': _L0_ffn_in['b1'], 'L0_ffn_W2': _L0_ffn_in['W2'], 'L0_ffn_b2': _L0_ffn_in['b2'], 'L0_ffn_ln1_g': _L0_ffn_in['ln1_g'], 'L0_ffn_ln1_b': _L0_ffn_in['ln1_b'], 'L0_ffn_ln2_g': _L0_ffn_in['ln2_g'], 'L0_ffn_ln2_b': _L0_ffn_in['ln2_b']}
    _x0 = _d['L0_attn_x']
    _d['L0_attn_x'] = jax.random.normal(jax.random.fold_in(jax.random.key(seed), 1), (1, 2048, 128), dtype=_x0.dtype)
    del _x0
    return _d

def reference(L0_attn_x, L0_attn_W_qkv, L0_attn_b_qkv, L0_attn_W_out, L0_attn_b_out, L0_ffn_Wq, L0_ffn_bq, L0_ffn_Wk, L0_ffn_bk, L0_ffn_Wv, L0_ffn_bv, L0_ffn_Wo, L0_ffn_bo, L0_ffn_router_w, L0_ffn_router_b, L0_ffn_W1, L0_ffn_b1, L0_ffn_W2, L0_ffn_b2, L0_ffn_ln1_g, L0_ffn_ln1_b, L0_ffn_ln2_g, L0_ffn_ln2_b):

    def _L0_attn_ref(x, W_qkv, b_qkv, W_out, b_out):
        import jax, jax.numpy as jnp
        import numpy as np
        B, S, DM = (2, 256, 128)
        H, D = (16, 64)

        def _rel_pos_enc(seq_len: int, dim: int) -> jnp.ndarray:
            positions = jnp.arange(seq_len, dtype=jnp.float32)[:, None]
            div_term = jnp.exp(jnp.arange(0, dim, 2, dtype=jnp.float32) * -(np.log(10000.0) / dim))
            pe = jnp.zeros((seq_len, dim), dtype=jnp.float32)
            pe = pe.at[:, 0::2].set(jnp.sin(positions * div_term))
            pe = pe.at[:, 1::2].set(jnp.cos(positions * div_term))
            return pe
        b, s, _ = x.shape
        qkv = x @ W_qkv + b_qkv
        qkv = qkv.reshape(b, s, 3, H, D)
        q, k, v = (qkv[:, :, 0], qkv[:, :, 1], qkv[:, :, 2])
        pos_enc = _rel_pos_enc(s, D)
        k = k + pos_enc[None, :, None, :]
        scale = jnp.sqrt(jnp.asarray(D, dtype=x.dtype))
        scores = jnp.einsum('bqhd,bkhd->bhqk', q, k) / scale
        attn = jax.nn.softmax(scores, axis=-1)
        out = jnp.einsum('bhqk,bkhd->bqhd', attn, v)
        out = out.reshape(b, s, H * D)
        return out @ W_out + b_out

    def _L0_ffn_ref(src, Wq, bq, Wk, bk, Wv, bv, Wo, bo, router_w, router_b, W1, b1, W2, b2, ln1_g, ln1_b, ln2_g, ln2_b):
        import jax, jax.numpy as jnp
        import numpy as np
        D_MODEL = 128
        N_HEAD = 16
        HEAD_DIM = D_MODEL // N_HEAD
        D_FF = 512
        N_EXPERTS = 4
        EPS = 1e-05

        def _layer_norm(x, gamma, beta):
            mu = jnp.mean(x, axis=-1, keepdims=True)
            var = jnp.mean((x - mu) ** 2, axis=-1, keepdims=True)
            return (x - mu) / jnp.sqrt(var + EPS) * gamma + beta
        B, T, _ = src.shape
        q = (src @ Wq + bq).reshape(B, T, N_HEAD, HEAD_DIM)
        k = (src @ Wk + bk).reshape(B, T, N_HEAD, HEAD_DIM)
        v = (src @ Wv + bv).reshape(B, T, N_HEAD, HEAD_DIM)
        scale = HEAD_DIM ** (-0.5)
        scores = jnp.einsum('bqhd,bkhd->bhqk', q, k) * scale
        probs = jax.nn.softmax(scores, axis=-1)
        attn = jnp.einsum('bhqk,bkhd->bqhd', probs, v).reshape(B, T, D_MODEL)
        attn = attn @ Wo + bo
        x = _layer_norm(src + attn, ln1_g, ln1_b)
        keys = (x @ router_w + router_b)[..., 0]
        expert_idx = jnp.remainder(jnp.floor(keys).astype(jnp.int32), N_EXPERTS)
        ff_out = jnp.zeros_like(x)
        for e in range(N_EXPERTS):
            h = jax.nn.relu(x @ W1[e] + b1[e])
            y = h @ W2[e] + b2[e]
            ff_out = ff_out + jnp.where((expert_idx == e)[..., None], y, 0.0)
        return _layer_norm(x + ff_out, ln2_g, ln2_b)
    x = L0_attn_x
    x = x + _L0_attn_ref(_layernorm(x, axis=-1), L0_attn_W_qkv, L0_attn_b_qkv, L0_attn_W_out, L0_attn_b_out)
    x = x + _L0_ffn_ref(_layernorm(x, axis=-1), L0_ffn_Wq, L0_ffn_bq, L0_ffn_Wk, L0_ffn_bk, L0_ffn_Wv, L0_ffn_bv, L0_ffn_Wo, L0_ffn_bo, L0_ffn_router_w, L0_ffn_router_b, L0_ffn_W1, L0_ffn_b1, L0_ffn_W2, L0_ffn_b2, L0_ffn_ln1_g, L0_ffn_ln1_b, L0_ffn_ln2_g, L0_ffn_ln2_b)
    return x

_drawn_inputs = setup_inputs


def setup_inputs(seed=0):
    import zlib

    import numpy as np

    out = dict(_drawn_inputs(seed))
    spreads = {'L0_attn_b_qkv': (0.0, 0.1),
     'L0_attn_b_out': (0.0, 0.1),
     'L0_ffn_bq': (0.0, 0.411),
     'L0_ffn_bk': (0.0, 0.8),
     'L0_ffn_bv': (0.0, 0.1),
     'L0_ffn_bo': (0.0, 0.1),
     'L0_ffn_b1': (0.0, 0.269),
     'L0_ffn_b2': (0.0, 0.1),
     'L0_ffn_ln1_g': (1.0, 0.2),
     'L0_ffn_ln1_b': (0.0, 0.1),
     'L0_ffn_ln2_g': (1.0, 0.2),
     'L0_ffn_ln2_b': (0.0, 0.1)}
    factors = {}
    for name, (base, spread) in spreads.items():
        noise = np.random.default_rng([zlib.crc32(name.encode()), seed]).standard_normal(out[name].shape)
        drawn = base * np.exp(spread * noise) if base else spread * noise
        out[name] = jnp.asarray(drawn.astype(out[name].dtype))
    for name, factor in factors.items():
        out[name] = (out[name] * factor).astype(out[name].dtype)
    return out
```

```python
from contextlib import ExitStack

import numpy as np

import concourse.bass as bass
from concourse import mybir

F32 = mybir.dt.float32
F32R = mybir.dt.float32r
I32 = mybir.dt.int32
ACT = mybir.ActivationFunctionType
ALU = mybir.AluOpType
AX = mybir.AxisListType

S = 2048
DM = 128
NT = S // 128
CW = 512
NC = S // CW
QT = CW // 128
EPS = 1e-5
H1, D1 = 16, 64
PAIRS = H1 // 2
STEPS1 = NT // 2
SCALE1 = D1 ** -0.5
H2, D2 = 16, 8
GROUPS = H2 // 4
STEPS2 = NT
SCALE2 = D2 ** -0.5
VW = 16
MROW = 3 * D2
E, FF = 4, 512
FT = FF // 128
LOADS1, LOADS3 = 6, 2 + 6 + E + 1
RING = 3


MAX1_STEPS = 6
EARLY1 = 4 * (STEPS1 - MAX1_STEPS)
TILES1 = [(h, q, k) for h in range(2) for q in range(QT) for k in range(NC)]


def side_items1(c):
    steps = [[] for _ in range(STEPS1)]
    for n, t in enumerate(TILES1[EARLY1:]):
        steps[n // 4].append(("max", *t))
    for n, t in enumerate(TILES1[:EARLY1]):
        steps[MAX1_STEPS + n // 4].append(("early", *t))
    for step, at, it in ((0, 1, ("acc7", 0)), (0, 3, ("acc7", 1)), (1, 1, ("accs", 0)), (1, 3, ("accs", 1)),
                         (3, 2, ("sums",)), (4, 3, ("y", 0)), (5, 3, ("y", 1))):
        steps[step].insert(at, it)
    steps[2].insert(2, ("Q",))
    for step, it in {0: [(4, ("K", 0)), (6, ("K", 1))], 1: [(4, ("K", 2)), (6, ("K", 3))],
                     2: [(3 + v, ("V", v)) for v in range(4)], 3: []}[c]:
        steps[step].append(it)
    steps[MAX1_STEPS].insert(0, ("mred",))
    steps[MAX1_STEPS].insert(2, ("fin",))
    steps[STEPS1 - 1].insert(2, ("acc6", 0))
    steps[STEPS1 - 1].append(("acc6", 1))
    return steps


END1 = [("acc7", 0), ("acc7", 1), ("accs", 0), ("accs", 1), ("sums",), ("y", 0), ("y", 1)]
DVE_ONLY = ("mred", "acc6", "acc7", "accs")


MAX2_STEPS = 13
EARLY2 = 4 * (STEPS2 - MAX2_STEPS)
TILES2 = [(h, q, k) for h in range(4) for q in range(QT) for k in range(NC)]


def side_items2(c, first):
    steps = [[] for _ in range(STEPS2)]
    for n, t in enumerate(TILES2[EARLY2:]):
        steps[n // 4].append(("max", *t))
    for n, t in enumerate(TILES2[:EARLY2]):
        steps[MAX2_STEPS + n // 4].append(("early", *t))
    steps[MAX2_STEPS].insert(0, ("mred",))
    steps[MAX2_STEPS].insert(3, ("fin",))
    if not first:
        steps[1].append(("o",))
    steps[3].append(("Q",))
    for step, it in {0: [(6, ("K", 0)), (10, ("K", 1))], 1: [(6, ("K", 2)), (10, ("K", 3))], 2: [(6, ("V",))], 3: []}[c]:
        steps[step].append(it)
    return steps


def on_pe(items):
    return [x for x in items if x[0] not in DVE_ONLY]


def uses_of(side_items, body, end=()):
    at, n = {}, 0
    for k in range(2 * NC):
        for items in side_items(k):
            for it in on_pe(items):
                at[(k, *it)] = n
                n += 1
    for it in on_pe(end):
        at[("end", *it)] = n
        n += 1
    assert n == body, (n, body)
    return at


def share(items, n):
    return [items[len(items) * k // n:len(items) * (k + 1) // n] for k in range(n)]


def build(nc, x, w_pairs, wout_pairs, bqk_pairs, bv_pairs, b_out, pos, w_groups, bqk_groups, bv_groups,
          coefs, w_o, b_o, router_w, router_b, w1, b1, w2, b2, ln1_g, ln1_b, ln2_g, ln2_b, identity, out):
    ctx = ExitStack()
    with ctx:
        def sb(name, shape, dt=F32):
            return ctx.enter_context(nc.sbuf_tensor(name, shape, dt))

        def sem(name):
            return ctx.enter_context(nc.semaphore(name))

        ka = sb("ka", [128, 2, 2, S], F32R)
        kb = sb("kb", [128, 2, 2, S], F32R)
        qa = sb("qa", [128, NC, 2, CW], F32R)
        qb = sb("qb", [128, NC, 2, CW], F32R)
        k4 = ka[:, :, 0, :]
        q4 = kb[:].rearrange("p a h n -> p (a h n)").rearrange("p (c h n) -> p c h n", c=NC, h=4)
        v1 = sb("v1", [128, 2, NT, 128])
        v1_flat = v1[:].rearrange("p a t n -> p (a t n)")
        v2_flat = v1_flat[:, 0:2 * NT * 4 * VW]
        v2 = v2_flat.rearrange("p (a t h n) -> p a t h n", a=2, t=NT, h=4)
        w1_sb = v1_flat[:, NT * 128:2 * NT * 128].rearrange("p (e n) -> p e n", e=E)
        prob = sb("prob", [128, 2, 4, 2, CW])
        accp = sb("accp", [128, 2, 2, CW])
        o2 = accp[:].rearrange("p a b n -> p (a b n)").rearrange("p (t n) -> p t n", t=NT)
        accs = sb("accs", [128, 2, CW])
        oraw = sb("oraw", [128, 2, CW])
        stage_q = sb("stage_q", [128, 2, CW], F32R)
        stage_kf = sb("stage_kf", [128, CW])
        stage_k = sb("stage_k", [128, 2, CW], F32R)
        pos_sb = sb("pos_sb", [128, S])
        s_sb = pos_sb[:].rearrange("p (t n) -> p t n", t=NT)
        x1 = sb("x1", [128, NT, DM])
        xnt = sb("xnt", [128, S])
        w_sb = sb("w_sb", [128, 2, 384])
        wout_sb = sb("wout_sb", [128, 2, DM])
        bqk_sb = sb("bqk_sb", [128, 2, 2])
        bv_sb = sb("bv_sb", [128, 2, 128])
        coef_sb = sb("coef_sb", [128, 4])
        ident = sb("ident", [128, 128])
        ones = sb("ones", [128, 1])
        zero = sb("zero", [128, 1])
        row_sb = sb("row_sb", [128, DM])
        mxp = sb("mxp", [128, 16, NC])
        mxp1 = [mxp[:, 0:8], mxp[:, 8:16]]
        mxp2 = [mxp, accs[:, 1, 0:16 * NC].rearrange("p (a b) -> p a b", a=16)]
        mx = sb("mx", [128, 16])
        m_rows = sb("m_rows", [16, 128], F32R)
        rs = sb("rs", [128, 16])
        stats = sb("stats", [128, NT, 6])
        credit = stats[:].rearrange("p t n -> p (t n)")
        mv = sb("mv", [128, NT, 2])
        std = sb("std", [128, NT])
        rstd = sb("rstd", [128, NT])
        prob_flat = prob[:].rearrange("p a r k n -> p (a r k n)")
        w2_sb = prob_flat[:, 0:2048].rearrange("p (e f n) -> p e f n", e=E, f=FT)
        hid = prob_flat[:, 2048:6144].rearrange("p (a f n) -> p a f n", a=2, f=FT)
        ff = prob_flat[:, 6144:8192].rearrange("p (t n) -> p t n", t=NT)
        xn_tok = prob_flat[:, 0:2048].rearrange("p (t n) -> p t n", t=NT)
        ot = v1_flat[:, 0:S]
        xt = xnt
        tail_rows = sb("tail_rows", [128, 6 + E, DM])
        b1_sb = sb("b1_sb", [128, E * FT])
        rb_sb = sb("rb_sb", [128, 1])
        wo_sb = sb("wo_sb", [128, DM])
        keys = sb("keys", [128, 4, NT])
        keys_i = sb("keys_i", [128, NT], I32)
        mask = sb("mask", [128, E, NT])

        sc = [ctx.enter_context(nc.psum_tensor(f"scores{h}", [128, 2, CW], F32)) for h in range(2)]
        acc_o = ctx.enter_context(nc.psum_tensor("acc_o", [128, CW], F32))
        ring = [ctx.enter_context(nc.psum_tensor(f"ring{n}", [128, CW], F32)) for n in range(RING)]

        ld = sem("ld")
        w_dma, wout_dma = sem("w_dma"), sem("wout_dma")
        side_full, side_free = sem("side_full"), sem("side_free")
        tokens_ready = sem("tokens_ready")
        var_ready, std_ready = sem("var_ready"), sem("std_ready")
        dve_own = sem("dve_own")
        sc_ready = [sem(f"sc_ready{h}") for h in range(2)]
        exp_done = [sem(f"exp_done{h}") for h in range(2)]
        pv_done = sem("pv_done")
        o_copied = sem("o_copied")
        pool_acc = [sem(f"pool_acc{h}") for h in range(2)]
        acc6_done = [sem(f"acc6_done{h}") for h in range(2)]
        acc7_done = [sem(f"acc7_done{h}") for h in range(2)]
        accs_done = [sem(f"accs_done{h}") for h in range(2)]
        mx_ready, m_dma = sem("mx_ready"), sem("m_dma")
        q_hi, q_dma = sem("q_hi"), sem("q_dma")
        kh_ready, k_ready, k_dma = sem("kh_ready"), sem("k_ready"), sem("k_dma")
        init2 = sem("init2")
        w2_dma = sem("w2_dma")
        sc2_ready = [sem(f"sc2_ready{h}") for h in range(2)]
        exp2_done = [sem(f"exp2_done{h}") for h in range(2)]
        pv2_done, o2_copied, rs2_ready = sem("pv2_done"), sem("o2_copied"), sem("rs2_ready")
        mx2_ready, m2_dma = sem("mx2_ready"), sem("m2_dma")
        q2_part, q2_ready, q2_dma = sem("q2_part"), sem("q2_ready"), sem("q2_dma")
        k2_part, k2_ready = sem("k2_part"), sem("k2_ready")
        ld3, w2_ld, hid_ready = sem("ld3"), sem("w2_ld"), sem("hid_ready")
        h_full, y_full, y_used = sem("h_full"), sem("y_full"), sem("y_used")
        out_ready, out_dma = sem("out_ready"), sem("out_dma")

        blank = sem("blank")
        from_one = [*exp_done, *exp2_done, o2_copied, *pool_acc, *acc6_done, y_used, y_full]

        PRO1 = NC + 2 + NC + NC + 8 * NC + 1 + EARLY1
        BODY1 = 2 * (NC * (8 * NC + 1 + 1 + 3) + 8)
        PRO2 = NC + 2 + NC + 1 + 16 * NC + 1 + EARLY2
        BODY2 = 2 * (NC * (16 * NC + 1 + 1 + 1) + 5)
        assert BODY1 % RING == 0 and BODY2 % RING == 0
        START1 = 0
        LOOP1 = START1 + PRO1
        ENDS1 = LOOP1 + BODY1 * (PAIRS // 2)
        START2 = ENDS1 + 3
        LOOP2 = START2 + PRO2
        START3 = LOOP2 + BODY2 * (GROUPS // 2)

        at1 = uses_of(lambda k: side_items1(k % NC), BODY1)
        at2 = uses_of(lambda k: side_items2(k % NC, k == 0), BODY2, [("o",)])

        def served1(i, k, *item):
            return LOOP1 + BODY1 * i + at1[(k, *item)] + 1

        def served2(i, k, *item):
            return LOOP2 + BODY2 * i + at2[(k, *item)] + 1

        def side_bank(static_use):
            return ring[static_use % RING]

        block = ctx.enter_context(nc.Block())

        @block.tensor
        def _(pe):
            use = [0, 0]

            def side(first=False):
                n = use[0] + use[1]
                bank = side_bank(use[1] + use[2])
                if not (isinstance(n, int) and n < RING):
                    pe.wait_ge(side_free, n - RING + 1)
                use[1] += 1
                return bank

            use.append(0)

            def rebase(base, static):
                use[0], use[1], use[2] = base, 0, static

            def transposes(norm, src):
                pe.wait_ge(tokens_ready, norm)
                for c in range(NC):
                    bank = side()
                    for q in range(QT):
                        last = nc.tensor.transpose(bank[:, q * 128:(q + 1) * 128], src[:, c * QT + q, :], ident[:])
                    last.then_inc(side_full, 1)

            def proj(par, col, src_lo):
                bank = side()
                nc.tensor.matmul(bank[:], w_sb[:, par, col * 128:(col + 1) * 128], xnt[:, src_lo:src_lo + CW],
                                 start=True, stop=True).then_inc(side_full, 1)

            def proj_v1(par, v):
                bank = side()
                for q in range(QT):
                    t = v * QT + q
                    last = nc.tensor.matmul(bank[:, q * 128:(q + 1) * 128], xnt[:, t * 128:(t + 1) * 128],
                                            w_sb[:, par, 256:384], start=True, stop=True)
                last.then_inc(side_full, 1)

            def proj_v2(par):
                bank = side()
                for t in range(NT):
                    last = nc.tensor.matmul(bank[:, t * 32:(t + 1) * 32], xnt[:, t * 128:(t + 1) * 128],
                                            w_sb[:, par, 256:288], start=True, stop=True)
                last.then_inc(side_full, 1)

            def max_tile1(par, c, h, q, k):
                bank = side()
                nc.tensor.matmul(bank[:], qa[:, c, h, q * 128:(q + 1) * 128], ka[:, par, h, k * CW:(k + 1) * CW],
                                 start=True, stop=True).then_inc(side_full, 1)

            def max_tile2(par, c, h, q, k):
                bank = side()
                nc.tensor.matmul(bank[:], q4[:, c, h, q * 128:(q + 1) * 128], k4[:, par, k * CW:(k + 1) * CW],
                                 start=True, stop=True).then_inc(side_full, 1)

            def fin(ready, count, n):
                bank = side()
                pe.wait_ge(ready, count)
                nc.tensor.transpose(bank[0:n, 0:128], mx[:, 0:n], ident[:]).then_inc(side_full, 1)

            rebase(START1, START1 % RING)
            pe.wait_ge(ld, 16 * LOADS1)
            transposes(1, xn_tok)
            pe.wait_ge(w_dma, 48)
            pe.wait_ge(side_free, START1 + NC)
            proj(0, 0, 0)
            proj(0, 0, CW)
            for c in range(NC):
                proj(0, 1, c * CW)
            for v in range(4):
                proj_v1(0, v)
            pe.wait_ge(q_dma, 96)
            pe.wait_ge(k_dma, 96 * NC)
            for t in TILES1:
                max_tile1(0, 0, *t)
            pe.wait_ge(q_dma, 192)
            for n, t in enumerate(TILES1[:EARLY1]):
                if n == 1:
                    fin(mx_ready, 1, 8)
                max_tile1(0, 1, *t)

            def scores1(G, par, c, h, j):
                pe.wait_ge(exp_done[h], 1 + STEPS1 * G + j)
                for k in range(2):
                    t = 2 * j + k
                    keys_of = slice(t * 128, (t + 1) * 128)
                    nc.tensor.matmul(sc[h][:, k, :], ka[:, par, h, keys_of], qa[:, c, h, :], start=True, stop=False)
                    last = nc.tensor.matmul(sc[h][:, k, :], kb[0:D1 + 1, par, h, keys_of], qb[0:D1 + 1, c, h, :],
                                            start=False, stop=True)
                last.then_inc(sc_ready[h], 1)

            def values1(G, par, j, k):
                t = 2 * j + k
                for h in range(2):
                    last = nc.tensor.matmul(acc_o[64 * h:64 * h + 64, :], v1[:, par, t, 64 * h:64 * h + 64],
                                            prob[:, h, j % 4, k, :], start=(t == 0), stop=(t == NT - 1))
                return last

            def sums1(ended):
                bank = side()
                for h in range(2):
                    pe.wait_ge(accs_done[h], 1 + ended)
                    for q in range(QT):
                        last = nc.tensor.matmul(bank[:, h * QT + q:h * QT + q + 1], accs[:, h, q * 128:(q + 1) * 128],
                                                ones[:], start=True, stop=True)
                last.then_inc(side_full, 1)

            def y1(ended, pairs_begun, par, k, h):
                bank = side()
                if h == 0:
                    pe.wait_ge(wout_dma, 16 * (pairs_begun + 1))
                    pe.wait_ge(o_copied, 1 + ended)
                for q in range(QT):
                    last = nc.tensor.matmul(bank[:, q * 128:(q + 1) * 128],
                                            oraw[64 * h:64 * h + 64, k % 2, q * 128:(q + 1) * 128],
                                            wout_sb[64 * h:64 * h + 64, par, :], start=True, stop=True)
                last.then_inc(side_full, 1)

            def item1(it, p, par, c, k, G):
                kind = it[0]
                if kind == "max":
                    max_tile1(par if c < 3 else 1 - par, (c + 1) % NC, *it[1:])
                elif kind == "early":
                    max_tile1(par if c < 2 else 1 - par, (c + 2) % NC, *it[1:])
                elif kind == "fin":
                    fin(mx_ready, G + 2, 8)
                elif kind == "Q":
                    proj(par if c < 2 else 1 - par, 0, ((c + 2) % NC) * CW)
                elif kind == "K":
                    if it[1] == 0:
                        pe.wait_ge(w_dma, 48 * (p + 2))
                    proj(1 - par, 1, it[1] * CW)
                elif kind == "V":
                    proj_v1(1 - par, it[1])
                elif kind == "sums":
                    sums1(G)
                elif kind == "y":
                    y1(G, *((p + 1, par) if c else (p, 1 - par)), k - 1, it[1])

            pe.wait_ge(m_dma, 32)
            scores1(0, 0, 0, 0, 0)
            scores1(0, 0, 0, 1, 0)
            with pe.Fori(0, PAIRS // 2) as i:
                rebase(LOOP1 + BODY1 * i, LOOP1 % RING)
                for k in range(2 * NC):
                    par, c = k // NC, k % NC
                    p = 2 * i + par
                    G = NC * p + c
                    for j, items in enumerate(side_items1(c)):
                        parts = share(on_pe(items), 3)
                        nxt = (G, par, c, j + 1) if j < STEPS1 - 1 else (G + 1, (k + 1) // NC % 2, (k + 1) % NC, 0)
                        if j == STEPS1 - 1:
                            pe.wait_ge(m_dma, 32 * (G + 2))
                        scores1(nxt[0], nxt[1], nxt[2], 0, nxt[3])
                        if j == MAX1_STEPS:
                            pe.wait_ge(q_dma, 96 * (G + 3))
                            if c == 2:
                                pe.wait_ge(k_dma, 96 * NC * (p + 2))
                        for it in parts[0]:
                            item1(it, p, par, c, k, G)
                        scores1(nxt[0], nxt[1], nxt[2], 1, nxt[3])
                        for it in parts[1]:
                            item1(it, p, par, c, k, G)
                        if j == 0:
                            pe.wait_ge(o_copied, 1 + G)
                        for h in range(2):
                            pe.wait_ge(exp_done[h], 1 + STEPS1 * G + j + 1)
                        values1(G, par, j, 0)
                        values1(G, par, j, 1).then_inc(pv_done, 1)
                        for it in parts[2]:
                            item1(it, p, par, c, k, G)
            rebase(ENDS1, ENDS1 % RING)
            sums1(NC * PAIRS)
            for h in range(2):
                y1(NC * PAIRS, PAIRS, 1, 2 * NC - 1, h)

            rebase(START2, START2 % RING)
            transposes(2, s_sb)
            pe.wait_ge(side_free, START2 + NC)
            pe.wait_ge(w2_dma, 48)
            proj(0, 0, 0)
            proj(0, 0, CW)
            for c in range(NC):
                proj(0, 1, c * CW)
            proj_v2(0)
            pe.wait_ge(q2_dma, 64)
            pe.wait_ge(k2_ready, NC)
            for t in TILES2:
                max_tile2(0, 0, *t)
            pe.wait_ge(q2_dma, 128)
            for n, t in enumerate(TILES2[:EARLY2]):
                if n == 2:
                    fin(mx2_ready, 1, 16)
                max_tile2(0, 1, *t)

            def scores2(G, par, c, u, t):
                pe.wait_ge(exp2_done[u], 1 + STEPS2 * G + t)
                for k in range(2):
                    last = nc.tensor.matmul(sc[u][:, k, :], k4[:, par, t * 128:(t + 1) * 128], q4[:, c, 2 * u + k, :],
                                            start=True, stop=True)
                last.then_inc(sc2_ready[u], 1)

            def values2(par, t, u):
                for k in range(2):
                    h = 2 * u + k
                    last = nc.tensor.matmul(acc_o[32 * h:32 * h + VW, :], v2[:, par, t, h, :],
                                            prob[:, u, t % 4, k, :], start=(t == 0), stop=(t == NT - 1))
                return last

            def o_rows(G, k):
                bank = side()
                pe.wait_ge(o2_copied, 1 + G + 1)
                for q in range(QT):
                    last = nc.tensor.transpose(bank[:, q * 128:(q + 1) * 128], oraw[:, k % 2, q * 128:(q + 1) * 128],
                                               ident[:])
                last.then_inc(side_full, 1)

            def item2(it, g, par, c, k, G):
                kind = it[0]
                if kind == "max":
                    max_tile2(par if c < 3 else 1 - par, (c + 1) % NC, *it[1:])
                elif kind == "early":
                    max_tile2(par if c < 2 else 1 - par, (c + 2) % NC, *it[1:])
                elif kind == "fin":
                    fin(mx2_ready, G + 2, 16)
                elif kind == "Q":
                    proj(par if c < 2 else 1 - par, 0, ((c + 2) % NC) * CW)
                elif kind == "K":
                    if it[1] == 0:
                        pe.wait_ge(w2_dma, 48 * (g + 2))
                    proj(1 - par, 1, it[1] * CW)
                elif kind == "V":
                    proj_v2(1 - par)
                elif kind == "o":
                    o_rows(G - 1, k - 1)

            def early_ready(g, c, G):
                pe.wait_ge(q2_dma, 64 * (G + 3))
                if c == 2:
                    pe.wait_ge(k2_ready, NC * (g + 2))

            with pe.Fori(0, GROUPS // 2) as i:
                rebase(LOOP2 + BODY2 * i, LOOP2 % RING)
                for k in range(2 * NC):
                    par, c = k // NC, k % NC
                    g = 2 * i + par
                    G = NC * g + c
                    if k == 0:
                        pe.wait_ge(m2_dma, 64 * (G + 1))
                        scores2(G, par, c, 0, 0)
                        scores2(G, par, c, 1, 0)
                    for t, items in enumerate(side_items2(c, k == 0)):
                        parts = share(on_pe(items), 4)
                        nxt = (G, par, c, t + 1) if t < STEPS2 - 1 else (G + 1, (k + 1) // NC, (k + 1) % NC, 0)
                        if t < STEPS2 - 1 or k < 2 * NC - 1:
                            if t == STEPS2 - 1:
                                pe.wait_ge(m2_dma, 64 * (G + 2))
                            scores2(nxt[0], nxt[1], nxt[2], 0, nxt[3])
                            if t == MAX2_STEPS:
                                early_ready(g, c, G)
                            for it in parts[0]:
                                item2(it, g, par, c, k, G)
                            scores2(nxt[0], nxt[1], nxt[2], 1, nxt[3])
                            for it in parts[1]:
                                item2(it, g, par, c, k, G)
                        else:
                            assert t != MAX2_STEPS
                            for it in parts[0] + parts[1]:
                                item2(it, g, par, c, k, G)
                        if t == 0:
                            pe.wait_ge(o2_copied, 1 + G)
                        for it in parts[2]:
                            item2(it, g, par, c, k, G)
                        for u in range(2):
                            pe.wait_ge(exp2_done[u], 1 + STEPS2 * G + t + 1)
                        values2(par, t, 0)
                        values2(par, t, 1).then_inc(pv2_done, 1)
                        for it in parts[3]:
                            item2(it, g, par, c, k, G)
                o_rows(G, k)

            rebase(START3, START3 % RING)
            pe.wait_ge(ld3, 16 * LOADS3)
            pe.wait_ge(side_free, START3)
            for c in range(NC):
                bank = side()
                for q in range(QT):
                    last = nc.tensor.transpose(bank[:, q * 128:(q + 1) * 128], o2[:, c * QT + q, :], ident[:])
                last.then_inc(side_full, 1)
            for c in range(NC):
                bank = side()
                pe.wait_ge(side_free, START3 + c + 1)
                for q in range(QT):
                    t = c * QT + q
                    last = nc.tensor.matmul(bank[:, q * 128:(q + 1) * 128], ot[:, t * 128:(t + 1) * 128], wo_sb[:],
                                            start=True, stop=True)
                last.then_inc(side_full, 1)
            transposes(3, s_sb)
            pe.wait_ge(side_free, START3 + 3 * NC)
            pe.wait_ge(w2_ld, 16 * E)

            def hidden(c, e):
                n = E * c + e
                for f in range(FT):
                    pe.wait_ge(hid_ready, FT * n + f + 1)
                    nc.tensor.matmul(sc[f % 2][:, f // 2, :], w1_sb[:, e, f * 128:(f + 1) * 128],
                                     xnt[:, bass.ds(CW * c, CW)], start=True, stop=True).then_inc(h_full, 1)

            def expert_out(c, e):
                n = E * c + e
                pe.wait_ge(y_used, 1 + n)
                pe.wait_ge(hid_ready, FT * (n + 2))
                for q in range(QT):
                    for f in range(FT):
                        last = nc.tensor.matmul(acc_o[:, q * 128:(q + 1) * 128],
                                                hid[:, e % 2, f, q * 128:(q + 1) * 128], w2_sb[:, e, f, :],
                                                start=(f == 0), stop=(f == FT - 1))
                last.then_inc(y_full, 1)

            with pe.Fori(0, NC) as c:
                hidden(c, 0)
                for e in range(E):
                    if e < E - 1:
                        hidden(c, e + 1)
                    expert_out(c, e)

        @block.scalar
        def _(act):
            def deviation(n):
                act.wait_ge(var_ready, n)
                nc.scalar.activation(std[:], std[:], ACT.Sqrt).then_inc(std_ready, 1)

            deviation(1)

            def exps1(G, h, j):
                act.wait_ge(sc_ready[h], STEPS1 * G + j + 1)
                act.wait_ge(pv_done, STEPS1 * G + j + 1)
                if j < 2:
                    act.wait_ge(pool_acc[h], 1 + 5 * G)
                elif j < 4:
                    act.wait_ge((acc6_done if j == 2 else acc7_done)[h], 1 + G)
                else:
                    act.wait_ge(pool_acc[h], 1 + 5 * G + max(j - 4, 1))
                nc.scalar.activation(prob[:, h, j % 4, :, :], sc[h][:, :, :], ACT.Exp, scale=SCALE1).then_inc(exp_done[h], 1)

            def copy_o1(i, ended, k):
                act.wait_ge(pv_done, STEPS1 * ended + 4)
                act.wait_ge(side_free, served1(i, k - 1, "y", 1) if k > 0 else LOOP1 + BODY1 * i)
                nc.scalar.activation(oraw[:, k % 2, :], acc_o[:], ACT.Copy).then_inc(o_copied, 1)

            with act.Fori(0, PAIRS // 2) as i:
                for k in range(2 * NC):
                    G = NC * 2 * i + k
                    for j in range(STEPS1):
                        exps1(G, 0, j)
                        exps1(G, 1, j)
                        if j == 0:
                            copy_o1(i, G, k - 1)
            copy_o1(PAIRS // 2 - 1, NC * PAIRS, 2 * NC - 1)

            def exps2(G, u, t):
                act.wait_ge(sc2_ready[u], STEPS2 * G + t + 1)
                act.wait_ge(pv2_done, STEPS2 * G + t + 1)
                nc.scalar.activation(prob[:, u, t % 4, :, :], sc[u][:, :, :], ACT.Exp, scale=SCALE2).then_inc(exp2_done[u], 1)

            def copy_o2(i, G, k):
                act.wait_ge(pv2_done, STEPS2 * (G + 1) + 4)
                act.wait_ge(side_free, LOOP2 + BODY2 * i if k < 2 else served2(i, k - 1, "o"))
                nc.scalar.activation(oraw[:, k % 2, :], acc_o[:], ACT.Copy).then_inc(o2_copied, 1)

            deviation(2)
            with act.Fori(0, GROUPS // 2) as i:
                for k in range(2 * NC):
                    G = NC * 2 * i + k
                    for t in range(STEPS2):
                        exps2(G, 0, t)
                        exps2(G, 1, t)
                        if t == 0 and k:
                            copy_o2(i, G - 1, k - 1)
                copy_o2(i, G, k)

            deviation(3)
            act.wait_ge(ld3, 16 * LOADS3)
            with act.Fori(0, NC) as c:
                for e in range(E):
                    n = E * c + e
                    if e == 0:
                        act.wait_ge(y_full, 1 + n)
                    elif e > 1:
                        act.wait_ge(y_full, 1 + n - 1)
                    for f in range(FT):
                        act.wait_ge(h_full, FT * n + f + 1)
                        nc.scalar.activation(hid[:, e % 2, f, :], sc[f % 2][:, f // 2, :], ACT.Relu,
                                             bias=b1_sb[:, e * FT + f:e * FT + f + 1]).then_inc(hid_ready, 1)
            deviation(4)

        @block.gpsimd
        def _(pool):
            def split_keys(n, served):
                pool.wait_ge(side_free, served)
                if not (isinstance(n, int) and n == 0):
                    pool.wait_ge(k_dma, 96 * n)
                nc.gpsimd.tensor_tensor(stage_k[:, 0, :], stage_kf[:], zero[:].to_broadcast([128, CW]), ALU.subtract).then_inc(kh_ready, 1)
                pool.wait_ge(kh_ready, n + 1)
                nc.gpsimd.tensor_tensor(stage_k[:, 1, :], stage_kf[:], stage_k[:, 0, :].bitcast(F32),
                                        ALU.subtract).then_inc(k_ready, 1)

            nc.gpsimd.memset(prob[:, :, 3], 1.0).then_inc(blank, 1)
            nc.gpsimd.memset(accp[:], 1.0).then_inc(blank, 1)
            for n in range(NC):
                split_keys(n, START1 + NC + 2 + n + 1)

            def add1(G, h, j):
                pool.wait_ge(exp_done[h], 1 + STEPS1 * G + j + 1)
                if j == 1:
                    pool.wait_ge(accs_done[h], 1 + G)
                    nc.gpsimd.tensor_tensor(accp[:, h], prob[:, h, 0], prob[:, h, 1], ALU.add).then_inc(pool_acc[h], 1)
                else:
                    pool.wait_ge(pool_acc[h], 1 + 5 * G + j - 1)
                    nc.gpsimd.tensor_tensor(accp[:, h], accp[:, h], prob[:, h, j % 4], ALU.add).then_inc(pool_acc[h], 1)

            with pool.Fori(0, PAIRS // 2) as i:
                for k in range(2 * NC):
                    p, c = 2 * i + k // NC, k % NC
                    G = NC * 2 * i + k
                    for j in range(1, 6):
                        add1(G, 0, j)
                        add1(G, 1, j)
                        if c < 2 and j >= 4:
                            b = 2 * c + j - 4
                            split_keys(NC * (p + 1) + b, served1(i, k, "K", b))

            pool.wait_ge(side_free, START2)
            pool.wait_ge(m_dma, 32 * (NC * PAIRS + 1))
            pool.wait_ge(q_dma, 96 * (NC * PAIRS + 2))
            pool.wait_ge(k_dma, 96 * NC * (PAIRS + 1))
            nc.gpsimd.memset(kb[:].rearrange("p a h n -> p (a h n)").bitcast(F32), 0.0).then_inc(init2, 1)
            nc.gpsimd.memset(v2_flat, 0.0).then_inc(init2, 1)
            pool.wait_ge(init2, 2)
            nc.gpsimd.memset(v2_flat.rearrange("p (x n) -> p x n", n=VW)[:, :, D2:D2 + 1], 1.0).then_inc(init2, 1)

        @block.sync
        def _(sp):
            x_t = x.rearrange("(t p) n -> p t n", p=128)
            sp.dma_start(x1[:], x_t).then_inc(ld, 16)
            sp.dma_start(ident[:], identity).then_inc(ld, 16)

            def load_pair(p, par, first=False):
                sp.dma_start(w_sb[:, par, :], w_pairs[bass.ds(p, 1), :, :].rearrange("a k n -> (a k) n")).then_inc(w_dma, 16)
                sp.dma_start(bqk_sb[:, par, :], bqk_pairs[bass.ds(p, 1), :, :].rearrange("a k n -> (a k) n")).then_inc(w_dma, 16)
                sp.dma_start(bv_sb[:, par, :], bv_pairs[bass.ds(p, 1), :].to_broadcast([128, 128])).then_inc(w_dma, 16)

            def load_wout(p, par):
                sp.dma_start(wout_sb[:, par, :], wout_pairs[bass.ds(p, 1), :, :].rearrange("a k n -> (a k) n")).then_inc(wout_dma, 16)

            load_pair(0, 0)
            sp.dma_start(pos_sb[:], pos).then_inc(ld, 16)
            sp.dma_start(row_sb[:], b_out[None, :].to_broadcast([128, DM])).then_inc(ld, 16)
            sp.dma_start(coef_sb[:], coefs).then_inc(ld, 16)
            sp.dma_start(b1_sb[:], b1).then_inc(ld, 16)
            sp.wait_ge(w_dma, 48)
            load_pair(1, 1)
            load_wout(1, 1)
            sp.wait_ge(wout_dma, 16)
            load_wout(0, 0)

            def move_q(c, served):
                sp.wait_ge(side_free, served)
                for h in range(2):
                    half = slice(64 * h, 64 * h + 64)
                    for to in range(2):
                        sp.dma_start(qa[64 * to:64 * to + 64, c, h, :].bitcast(F32), stage_q[half, 0, :].bitcast(F32)).then_inc(q_dma, 16)
                    sp.dma_start(qb[0:64, c, h, :].bitcast(F32), stage_q[half, 1, :].bitcast(F32)).then_inc(q_dma, 16)

            def move_k(n, par, c):
                sp.wait_ge(k_ready, n + 1)
                cols = slice(c * CW, (c + 1) * CW)
                for h in range(2):
                    half = slice(64 * h, 64 * h + 64)
                    sp.dma_start(ka[0:64, par, h, cols].bitcast(F32), stage_k[half, 0, :].bitcast(F32)).then_inc(k_dma, 16)
                    sp.dma_start(ka[64:128, par, h, cols].bitcast(F32), stage_k[half, 1, :].bitcast(F32)).then_inc(k_dma, 16)
                    sp.dma_start(kb[0:64, par, h, cols].bitcast(F32), stage_k[half, 0, :].bitcast(F32)).then_inc(k_dma, 16)

            def move_m(c, served):
                sp.wait_ge(side_free, served)
                for h in range(2):
                    sp.dma_start(qb[D1:D1 + 1, c, h, :].bitcast(F32), m_rows[QT * h:QT * (h + 1), :].bitcast(F32)).then_inc(m_dma, 16)

            move_q(0, START1 + NC + 1)
            move_q(1, START1 + NC + 2)
            for c in range(NC):
                move_k(c, 0, c)
            move_m(0, START1 + PRO1 - (EARLY1 - 1))
            with sp.Fori(0, PAIRS // 2) as i:
                for k in range(2 * NC):
                    par, c = k // NC, k % NC
                    p = 2 * i + par
                    G = NC * p + c
                    move_q((c + 2) % NC, served1(i, k, "Q"))
                    if c < 2:
                        move_k(NC * (p + 1) + 2 * c, 1 - par, 2 * c)
                    if c == 2:
                        load_pair(p + 2, par)
                        sp.wait_ge(side_free, served1(i, k - 1, "fin"))
                        load_wout(p + 1, 1 - par)
                    move_m((c + 1) % NC, served1(i, k, "fin"))
                    if c < 2:
                        move_k(NC * (p + 1) + 2 * c + 1, 1 - par, 2 * c + 1)

            def load_group(g, par):
                sp.dma_start(w_sb[:, par, 0:288], w_groups[bass.ds(g, 1), :, :].rearrange("a k n -> (a k) n")).then_inc(w2_dma, 16)
                sp.dma_start(bqk_sb[:, par, :], bqk_groups[bass.ds(g, 1), :, :].rearrange("a k n -> (a k) n")).then_inc(w2_dma, 16)
                sp.dma_start(bv_sb[:, par, 0:32], bv_groups[bass.ds(g, 1), :].to_broadcast([128, 32])).then_inc(w2_dma, 16)

            sp.wait_ge(side_free, START2)
            sp.wait_ge(w_dma, 48 * (PAIRS + 2))
            sp.wait_ge(wout_dma, 16 * (PAIRS + 2))
            load_group(0, 0)
            sp.wait_ge(w2_dma, 48)
            load_group(1, 1)
            sp.dma_start(w1_sb, w1.rearrange("e k n -> k e n")).then_inc(ld3, 16)
            sp.dma_start(wo_sb[:], w_o).then_inc(ld3, 16)
            for n, src in enumerate((b_o, ln1_g, ln1_b, ln2_g, ln2_b, router_w)):
                sp.dma_start(tail_rows[:, n, :], src[None, :].to_broadcast([128, DM])).then_inc(ld3, 16)
            for e in range(E):
                sp.dma_start(tail_rows[:, 6 + e, :], b2[e:e + 1, :].to_broadcast([128, DM])).then_inc(ld3, 16)
            sp.dma_start(rb_sb[:], router_b[None, :].to_broadcast([128, 1])).then_inc(ld3, 16)

            def move_q2(n, c):
                sp.wait_ge(q2_ready, n + 1)
                for h in range(4):
                    rows = slice(32 * h, 32 * h + 32)
                    sp.dma_start(q4[rows, c, h, :].bitcast(F32), stage_q[rows, 0, :].bitcast(F32)).then_inc(q2_dma, 16)

            def move_m2(c, served):
                sp.wait_ge(side_free, served)
                for h in range(4):
                    sp.dma_start(q4[32 * h + MROW:32 * h + MROW + 1, c, h, :].bitcast(F32), m_rows[QT * h:QT * (h + 1), :].bitcast(F32)).then_inc(m2_dma, 16)

            sp.wait_ge(init2, 3)
            move_q2(0, 0)
            move_q2(1, 1)
            move_m2(0, START2 + PRO2 - (EARLY2 - 2))
            with sp.Fori(0, GROUPS // 2) as i:
                for k in range(2 * NC):
                    par, c = k // NC, k % NC
                    g = 2 * i + par
                    G = NC * g + c
                    move_q2(G + 2, (c + 2) % NC)
                    if c == 2:
                        load_group(g + 2, par)
                    move_m2((c + 1) % NC, served2(i, k, "fin"))
            sp.wait_ge(side_free, START3)
            sp.wait_ge(m2_dma, 64 * (NC * GROUPS + 1))
            sp.wait_ge(q2_dma, 64 * (NC * GROUPS + 2))
            sp.wait_ge(w2_dma, 48 * (GROUPS + 2))
            for e in range(E):
                sp.dma_start(w2_sb[:, e], w2[e].rearrange("(f k) n -> k f n", k=128)).then_inc(w2_ld, 16)
            out_t = out.rearrange("(t p) n -> p t n", p=128)
            for c in range(NC):
                sp.wait_ge(out_ready, c + 1)
                sp.dma_start(out_t[:, c * QT:(c + 1) * QT, :], ff[:, c * QT:(c + 1) * QT, :]).then_inc(out_dma, 16)
            sp.wait_ge(out_dma, 16 * NC)

        @block.vector
        def _(dve):
            use = [0, 0, 0]
            own = [0]

            def link(ins):
                own[0] += 1
                ins.then_inc(dve_own, 1)
                dve.wait_ge(dve_own, own[0])

            def rebase(base, static):
                use[0], use[1], use[2] = base, 0, static

            def side():
                bank = side_bank(use[1] + use[2])
                use[1] += 1
                dve.wait_ge(side_full, use[0] + use[1])
                return bank

            def norm(n, dst, src, affine=None):
                for t in range(NT):
                    last = nc.vector.bn_stats(stats[:, t, :], src[:, t, :])
                link(last)
                for t in range(NT):
                    last = nc.vector.bn_aggr(mv[:, t, :], stats[:, t, :])
                link(last)
                nc.vector.tensor_scalar(std[:], mv[:, :, 1], EPS, None, ALU.add).then_inc(var_ready, 1)
                dve.wait_ge(std_ready, n)
                link(nc.vector.reciprocal(rstd[:], std[:]))
                for t in range(NT):
                    last = nc.vector.tensor_scalar(dst[:, t, :], src[:, t, :], mv[:, t, 0:1], rstd[:, t:t + 1],
                                                   ALU.subtract, ALU.mult)
                if affine is not None:
                    link(last)
                    link(nc.vector.tensor_tensor(dst[:], dst[:], all_tokens(affine[0]), ALU.mult))
                    last = nc.vector.tensor_tensor(dst[:], dst[:], all_tokens(affine[1]), ALU.add)
                return last

            def all_tokens(row):
                return tail_rows[:, row:row + 1, :].to_broadcast([128, NT, DM])

            def copy_transposed(dst):
                for c in range(NC):
                    bank = side()
                    nc.vector.tensor_copy(dst[:, c * CW:(c + 1) * CW], bank[:]).then_inc(side_free, 1)

            for par in range(2):
                for h in range(2):
                    last = nc.vector.memset(kb[D1:D1 + 1, par, h, :].bitcast(F32), 1.0)
            link(last)
            link(nc.vector.memset(ones[:], 1.0))
            link(nc.vector.memset(zero[:], 0.0))
            nc.vector.memset(credit[:, 0:1], 0.0).then_inc(pv_done, 4)
            nc.vector.memset(credit[:, 1:2], 0.0).then_inc(pv2_done, 4)
            nc.vector.memset(credit[:, 2:3], 0.0).then_inc(hid_ready, FT)
            for n, s in enumerate(from_one):
                nc.vector.memset(credit[:, 3 + n:4 + n], 0.0).then_inc(s, 1)
            link(nc.vector.memset(credit[:, 40:41], 0.0))
            dve.wait_ge(ld, 16 * LOADS1)
            rebase(START1, START1 % RING)
            norm(1, xn_tok, x1).then_inc(tokens_ready, 1)
            copy_transposed(xnt)
            link(nc.vector.tensor_tensor(x1[:], x1[:], row_sb[:].rearrange("p (a n) -> p a n", a=1)
                                         .to_broadcast([128, NT, DM]), ALU.add))

            def done_so_far():
                dve.wait_ge(side_free, use[0] + use[1])

            def q_proj(n, par):
                if not (isinstance(n, int) and n == 0):
                    dve.wait_ge(q_dma, 96 * n)
                bank = side()
                bias = bqk_sb[:, par, 0:1]
                nc.vector.tensor_scalar(stage_q[:, 0, :], bank[:], bias, None, ALU.add).then_inc(q_hi, 1)
                dve.wait_ge(q_hi, n + 1)
                nc.vector.scalar_tensor_tensor(stage_q[:, 1, :], bank[:], bias, stage_q[:, 0, :].bitcast(F32),
                                               ALU.add, ALU.subtract).then_inc(side_free, 1)

            def k_proj(n, par, c):
                if not (isinstance(n, int) and n == 0):
                    dve.wait_ge(k_ready, n)
                bank = side()
                nc.vector.scalar_tensor_tensor(stage_kf[:], bank[:], bqk_sb[:, par, 1:2], pos_sb[:, c * CW:(c + 1) * CW],
                                               ALU.add, ALU.add).then_inc(side_free, 1)

            def v_proj(par, v):
                bank = side()
                nc.vector.tensor_tensor(v1[:, par, v * QT:(v + 1) * QT, :], bank[:].rearrange("p (t n) -> p t n", t=QT),
                                        bv_sb[:, par:par + 1, :].to_broadcast([128, QT, 128]), ALU.add).then_inc(side_free, 1)

            def max_tile(h, q, k, partial):
                bank = side()
                nc.vector.reduce_max(partial[:, h * QT + q, k:k + 1], bank[:], AX.X).then_inc(side_free, 1)

            def mred(heads, ready, partial):
                done_so_far()
                nc.vector.reduce_max(mx[:, 0:heads * QT], partial[:, 0:heads * QT, :], AX.X).then_inc(ready, 1)

            def fin(n, heads, moved):
                if not (isinstance(n, int) and n == 0):
                    dve.wait_ge(moved, 16 * heads * n)
                bank = side()
                nc.vector.tensor_scalar(m_rows[0:heads * QT, :], bank[0:heads * QT, 0:128], -1.0, None,
                                        ALU.mult).then_inc(side_free, 1)

            link(nc.vector.memset(acc_o[:], 0.0))
            dve.wait_ge(blank, 2)
            dve.wait_ge(w_dma, 48)
            q_proj(0, 0)
            q_proj(1, 0)
            for c in range(NC):
                k_proj(c, 0, c)
            for v in range(4):
                v_proj(0, v)
            for t in TILES1:
                max_tile(*t, mxp1[0])
            mred(2, mx_ready, mxp1[0])
            for n, t in enumerate(TILES1[:EARLY1]):
                if n == 1:
                    fin(0, 2, m_dma)
                max_tile(*t, mxp1[1])

            def add_last(h, j, done):
                nc.vector.tensor_tensor(accp[:, h], accp[:, h], prob[:, h, j % 4], ALU.add).then_inc(done[h], 1)

            def item1(it, p, par, c, k, G):
                kind = it[0]
                last_k = k - 1
                if kind == "max":
                    max_tile(*it[1:], mxp1[(k + 1) % 2])
                elif kind == "early":
                    max_tile(*it[1:], mxp1[k % 2])
                elif kind == "mred":
                    mred(2, mx_ready, mxp1[(k + 1) % 2])
                elif kind == "fin":
                    fin(G + 1, 2, m_dma)
                elif kind == "Q":
                    q_proj(G + 2, par if c < 2 else 1 - par)
                elif kind == "K":
                    if it[1] == 0:
                        dve.wait_ge(w_dma, 48 * (p + 2))
                    k_proj(NC * (p + 1) + it[1], 1 - par, it[1])
                elif kind == "V":
                    v_proj(1 - par, it[1])
                elif kind == "acc6":
                    h = it[1]
                    dve.wait_ge(exp_done[h], 1 + STEPS1 * G + 7)
                    dve.wait_ge(pool_acc[h], 1 + 5 * (G + 1))
                    add_last(h, 6, acc6_done)
                else:
                    end1(it, G, (c - 1) % NC)

            def end1(it, ended, c):
                kind = it[0]
                if kind == "acc7":
                    h = it[1]
                    dve.wait_ge(exp_done[h], 1 + STEPS1 * ended)
                    dve.wait_ge(acc6_done[h], 1 + ended)
                    add_last(h, 7, acc7_done)
                elif kind == "accs":
                    h = it[1]
                    dve.wait_ge(acc7_done[h], 1 + ended)
                    nc.vector.tensor_tensor(accs[:, h, :], accp[:, h, 0, :], accp[:, h, 1, :], ALU.add).then_inc(accs_done[h], 1)
                elif kind == "sums":
                    bank = side()
                    nc.vector.reciprocal(rs[:, 0:2 * QT], bank[:, 0:2 * QT]).then_inc(side_free, 1)
                elif kind == "y":
                    h = it[1]
                    done_so_far()
                    bank = side()
                    for q in range(QT):
                        t = c * QT + q
                        last = nc.vector.scalar_tensor_tensor(x1[:, t, :], bank[:, q * 128:(q + 1) * 128],
                                                              rs[:, h * QT + q:h * QT + q + 1], x1[:, t, :],
                                                              ALU.mult, ALU.add)
                    last.then_inc(side_free, 1)

            with dve.Fori(0, PAIRS // 2) as i:
                rebase(LOOP1 + BODY1 * i, LOOP1 % RING)
                for k in range(2 * NC):
                    par, c = k // NC, k % NC
                    p = 2 * i + par
                    G = NC * p + c
                    for items in side_items1(c):
                        for it in items:
                            item1(it, p, par, c, k, G)
            rebase(ENDS1, ENDS1 % RING)
            for it in END1:
                end1(it, NC * PAIRS, NC - 1)

            rebase(START2, START2 % RING)
            dve.wait_ge(side_free, START2)
            norm(2, s_sb, x1).then_inc(tokens_ready, 1)
            copy_transposed(xnt)
            dve.wait_ge(w2_dma, 48)

            def parts2(bank, bias, col, hi, mixed, part, part_count):
                nc.vector.tensor_scalar(hi, bank[:], bias, None, ALU.add).then_inc(part, 1)
                nc.vector.tensor_scalar(mixed, bank[:], bias, coef_sb[:, col:col + 1], ALU.add, ALU.mult).then_inc(side_free, 1)
                dve.wait_ge(part, part_count)
                done_so_far()

            def q2_proj(n, par):
                if not (isinstance(n, int) and n == 0):
                    dve.wait_ge(q2_ready, n)
                bank = side()
                parts2(bank, bqk_sb[:, par, 0:1], 0, stage_q[:, 1, :], accs[:, 0, :], q2_part, n + 1)
                if not (isinstance(n, int) and n == 0):
                    dve.wait_ge(q2_dma, 64 * n)
                nc.vector.scalar_tensor_tensor(stage_q[:, 0, :], stage_q[:, 1, :].bitcast(F32), coef_sb[:, 1:2],
                                               accs[:, 0, :], ALU.mult, ALU.add).then_inc(q2_ready, 1)

            def k2_proj(n, par, c):
                if not (isinstance(n, int) and n == 0):
                    dve.wait_ge(k2_ready, n)
                bank = side()
                parts2(bank, bqk_sb[:, par, 1:2], 2, stage_k[:, 0, :], stage_kf[:], k2_part, n + 1)
                nc.vector.scalar_tensor_tensor(k4[:, par, c * CW:(c + 1) * CW], stage_k[:, 0, :].bitcast(F32),
                                               coef_sb[:, 3:4], stage_kf[:], ALU.mult, ALU.add).then_inc(k2_ready, 1)

            def v2_proj(par):
                bank = side()
                nc.vector.tensor_tensor(v2[:, par, :, :, 0:D2], bank[:].rearrange("p (t h n) -> p t h n", t=NT, h=4),
                                        bv_sb[:, par, 0:32].rearrange("p (a h n) -> p a h n", a=1, h=4)
                                        .to_broadcast([128, NT, 4, D2]), ALU.add).then_inc(side_free, 1)

            q2_proj(0, 0)
            q2_proj(1, 0)
            for c in range(NC):
                k2_proj(c, 0, c)
            dve.wait_ge(init2, 3)
            v2_proj(0)
            for t in TILES2:
                max_tile(*t, mxp2[0])
            mred(4, mx2_ready, mxp2[0])
            for n, t in enumerate(TILES2[:EARLY2]):
                if n == 2:
                    fin(0, 4, m2_dma)
                max_tile(*t, mxp2[1])

            def o_rows(G, g, c):
                bank = side()
                rows = bank[:].rearrange("p (t h r) -> p t h r", t=QT, h=4)
                nc.vector.reciprocal(rs[:].rearrange("p (t h a) -> p t h a", t=QT, h=4), rows[:, :, :, D2:D2 + 1]).then_inc(rs2_ready, 1)
                dve.wait_ge(rs2_ready, G + 1)
                nc.vector.tensor_tensor(o2[:, c * QT:(c + 1) * QT, bass.ds(32 * g, 32)].rearrange("p t (h n) -> p t h n", h=4),
                                        rows[:, :, :, 0:D2],
                                        rs[:].rearrange("p (t h a) -> p t h a", t=QT, h=4).to_broadcast([128, QT, 4, D2]),
                                        ALU.mult).then_inc(side_free, 1)

            with dve.Fori(0, GROUPS // 2) as i:
                rebase(LOOP2 + BODY2 * i, LOOP2 % RING)
                for k in range(2 * NC):
                    par, c = k // NC, k % NC
                    g = 2 * i + par
                    G = NC * g + c
                    for items in side_items2(c, k == 0):
                        for it in items:
                            kind = it[0]
                            if kind == "max":
                                max_tile(*it[1:], mxp2[(k + 1) % 2])
                            elif kind == "early":
                                max_tile(*it[1:], mxp2[k % 2])
                            elif kind == "mred":
                                mred(4, mx2_ready, mxp2[(k + 1) % 2])
                            elif kind == "fin":
                                fin(G + 1, 4, m2_dma)
                            elif kind == "Q":
                                q2_proj(G + 2, par if c < 2 else 1 - par)
                            elif kind == "K":
                                if it[1] == 0:
                                    dve.wait_ge(w2_dma, 48 * (g + 2))
                                k2_proj(NC * (g + 1) + it[1], 1 - par, it[1])
                            elif kind == "V":
                                v2_proj(1 - par)
                            else:
                                o_rows(G - 1, g if c else g - 1, (c - 1) % NC)
                o_rows(G, g, c)

            rebase(START3, START3 % RING)
            dve.wait_ge(ld3, 16 * LOADS3)
            dve.wait_ge(side_free, START3)
            copy_transposed(ot)
            for c in range(NC):
                bank = side()
                tiles = slice(c * QT, (c + 1) * QT)
                nc.vector.tensor_tensor(s_sb[:, tiles, :], s_sb[:, tiles, :], bank[:].rearrange("p (t n) -> p t n", t=QT),
                                        ALU.add).then_inc(side_free, 1)
            done_so_far()
            link(nc.vector.tensor_tensor(s_sb[:], s_sb[:], all_tokens(0), ALU.add))
            norm(3, s_sb, s_sb, affine=(1, 2)).then_inc(tokens_ready, 1)
            copy_transposed(xnt)
            dve.wait_ge(tokens_ready, 3)

            link(nc.vector.tensor_tensor(ff[:], s_sb[:], all_tokens(5), ALU.mult))
            link(nc.vector.reduce_sum(keys[:, 0, :], ff[:], AX.X))
            link(nc.vector.tensor_scalar(keys[:, 0, :], keys[:, 0, :], rb_sb[:, 0:1], None, ALU.add))

            def floor(dst, src, tmp):
                link(nc.vector.tensor_copy(keys_i[:], src))
                link(nc.vector.tensor_copy(dst, keys_i[:]))
                link(nc.vector.tensor_tensor(tmp, dst, src, ALU.is_gt))
                link(nc.vector.tensor_tensor(dst, dst, tmp, ALU.subtract))

            floor(keys[:, 1, :], keys[:, 0, :], keys[:, 3, :])
            link(nc.vector.tensor_scalar(keys[:, 0, :], keys[:, 1, :], 1.0 / E, None, ALU.mult))
            floor(keys[:, 2, :], keys[:, 0, :], keys[:, 3, :])
            link(nc.vector.scalar_tensor_tensor(keys[:, 0, :], keys[:, 2, :], -float(E), keys[:, 1, :], ALU.mult, ALU.add))
            for e in range(E):
                last = nc.vector.tensor_scalar(mask[:, e, :], keys[:, 0, :], float(e), None, ALU.is_equal)
            link(last)
            for e in range(E):
                for t in range(NT):
                    last = nc.vector.scalar_tensor_tensor(ff[:, t, :], tail_rows[:, 6 + e, :], mask[:, e, t:t + 1],
                                                          (ff if e else s_sb)[:, t, :], ALU.mult, ALU.add)
                link(last)

            with dve.Fori(0, NC) as c:
                for e in range(E):
                    n = E * c + e
                    dve.wait_ge(y_full, 1 + n + 1)
                    dve.wait_ge(y_used, 1 + n)
                    for q in range(QT):
                        t = bass.ds(QT * c + q, 1)
                        tok = ff[:, t, :].rearrange("p a n -> p (a n)")
                        last = nc.vector.scalar_tensor_tensor(tok, acc_o[:, q * 128:(q + 1) * 128], mask[:, e, t], tok,
                                                              ALU.mult, ALU.add)
                    last.then_inc(y_used, 1)
            dve.wait_ge(y_used, 1 + E * NC)
            link(norm(4, ff, ff, affine=(3, 4)))
            for c in range(NC):
                tiles = slice(c * QT, (c + 1) * QT)
                nc.vector.tensor_tensor(ff[:, tiles, :], ff[:, tiles, :], x1[:, tiles, :], ALU.add).then_inc(out_ready, 1)


def positions():
    f = np.float32
    freq = np.exp((np.arange(0, D1, 2, dtype=f) * f(-(np.log(10000.0) / D1))).astype(np.float64)).astype(f)
    angle = np.arange(S, dtype=f)[:, None] * freq
    pe = np.zeros((S, D1), f)
    pe[:, 0::2] = np.sin(angle.astype(np.float64))
    pe[:, 1::2] = np.cos(angle.astype(np.float64))
    return np.ascontiguousarray(np.tile(pe.T, (2, 1)))


def coefficients():
    out = np.zeros((128, 4), np.float32)
    for h in range(4):
        r = 32 * h
        out[r:r + 2 * D2, 1] = 1
        out[r + 2 * D2:r + 3 * D2, 0], out[r + 2 * D2:r + 3 * D2, 1] = 1, -1
        out[r:r + D2, 3] = 1
        out[r + D2:r + 2 * D2, 2], out[r + D2:r + 2 * D2, 3] = 1, -1
        out[r + 2 * D2:r + MROW + 1, 3] = 1
    return out


def kernel(**inputs):
    import concourse.bacc as bacc
    from concourse.bass_utils import run_bass_kernel_spmd

    a = {k: np.asarray(v) for k, v in inputs.items()}
    att = {k[8:]: v for k, v in a.items() if k.startswith("L0_attn_")}
    ffn = {k[7:]: v for k, v in a.items() if k.startswith("L0_ffn_")}
    f = np.float32

    pairs = [p % PAIRS for p in range(PAIRS + 2)]
    w = att["W_qkv"].reshape(DM, 3, PAIRS, 128)
    w_pairs = np.stack([w[:, :, p].reshape(DM, 384) for p in pairs])
    wout_pairs = np.stack([att["W_out"].reshape(PAIRS, 128, DM)[p] for p in pairs])
    b = att["b_qkv"].reshape(3, PAIRS, 128)
    bqk_pairs = np.stack([b[:2, p].T for p in pairs])
    bv_pairs = np.stack([b[2, p] for p in pairs])

    groups = [g % GROUPS for g in range(GROUPS + 2)]

    def thrice(cols, one):
        c = cols.reshape(-1, GROUPS, 4, D2)
        rows = np.zeros((c.shape[0], GROUPS, 4, 32), f)
        for n in range(3):
            rows[..., n * D2:(n + 1) * D2] = c
        rows[..., MROW] = one
        return rows.reshape(-1, GROUPS, 128)

    wq, wk = thrice(ffn["Wq"], 0), thrice(ffn["Wk"], 0)
    wv = ffn["Wv"].reshape(DM, GROUPS, 32)
    w_groups = np.stack([np.concatenate([wq[:, g], wk[:, g], wv[:, g]], 1) for g in groups])
    bq, bk = thrice(ffn["bq"], 0)[0], thrice(ffn["bk"], 1)[0]
    bqk_groups = np.stack([np.stack([bq[g], bk[g]], 1) for g in groups])
    bv_groups = np.stack([ffn["bv"].reshape(GROUPS, 32)[g] for g in groups])

    arrays = dict(
        x=att["x"].reshape(S, DM), w_pairs=w_pairs, wout_pairs=wout_pairs, bqk_pairs=bqk_pairs, bv_pairs=bv_pairs,
        b_out=att["b_out"], pos=positions(), w_groups=w_groups, bqk_groups=bqk_groups, bv_groups=bv_groups,
        coefs=coefficients(), w_o=ffn["Wo"], b_o=ffn["bo"], router_w=ffn["router_w"].reshape(DM),
        router_b=ffn["router_b"], w1=ffn["W1"], b1=ffn["b1"].reshape(E * FT, 128).T, w2=ffn["W2"], b2=ffn["b2"],
        ln1_g=ffn["ln1_g"], ln1_b=ffn["ln1_b"], ln2_g=ffn["ln2_g"], ln2_b=ffn["ln2_b"], identity=np.eye(128, dtype=f))
    arrays = {k: np.ascontiguousarray(v) for k, v in arrays.items()}

    nc = bacc.Bacc("TRN2", target_bir_lowering=False, num_devices=1)
    handles = {k: nc.dram_tensor(k, v.shape, mybir.dt.from_np(v.dtype), kind="ExternalInput").ap() for k, v in arrays.items()}
    out = nc.dram_tensor("out", [S, DM], F32, kind="ExternalOutput").ap()
    build(nc, out=out, **handles)
    r = run_bass_kernel_spmd(nc, [arrays], core_ids=[0])
    return r.results[0]["out"].reshape(1, S, DM)
```
